# Optimizing a Trainium2 kernel written in Bass

```python
import numpy as np
import jax
import jax.numpy as jnp

def _softmax(x, axis=-1):
    return jax.nn.softmax(x, axis=axis)

def _gelu(x):
    return jax.nn.gelu(x, approximate=True)

def _silu(x):
    return jax.nn.silu(x)

def _sigmoid(x):
    return jax.nn.sigmoid(x)

def _layernorm(x, axis=-1, eps=1e-05):
    m = jnp.mean(x, axis=axis, keepdims=True)
    v = jnp.var(x, axis=axis, keepdims=True)
    return (x - m) / jnp.sqrt(v + eps)

def _scatter_add(tgt, idx, src, axis=0):
    return tgt.at[idx].add(src)

def _segment_sum(src, seg, n):
    return jax.ops.segment_sum(src, seg, n)
kernel_name = 'mk_gnn_preln_d4_gnn_r32_5735fd'

def setup_inputs(seed: int=0):
    np.random.seed(seed)
    _w = jnp.asarray

    def _rec_inputs():
        import jax
        import jax.numpy as jnp
        _gk = jax.random.key(seed)
        x = -0.000202 + 1 * jax.random.normal(jax.random.fold_in(_gk, 1), (3125, 128), jnp.float32)
        src = jax.random.randint(jax.random.fold_in(_gk, 2), (100000,), 0, 3125, jnp.int32)
        dst = jax.random.randint(jax.random.fold_in(_gk, 3), (100000,), 0, 3125, jnp.int32)
        _o = jnp.argsort(dst, stable=True)
        src = src[_o]
        dst = dst[_o]
        edge_weight = jax.random.uniform(jax.random.fold_in(_gk, 14), (100000,), jnp.float32, 0.0, 0.999999)
        edge_weight_n2 = jax.random.uniform(jax.random.fold_in(_gk, 15), (100000,), jnp.float32, 0.0, 0.999999)
        edge_weight1 = 0.000937891 + 0.999965 * jax.random.normal(jax.random.fold_in(_gk, 16), (100000, 1), jnp.float32)
        return (x, src, dst, edge_weight, edge_weight_n2, edge_weight1)
    x, src, dst, edge_weight, edge_weight_n2, edge_weight1 = _rec_inputs()

    def _L0_gnn_setup():
        import jax, jax.numpy as jnp
        import numpy as np
        N_NODES = 50000
        N_EDGES = 50000
        IN_F = 128
        HID = 128
        N_CLASSES = 128

        def _glorot(key, shape):
            lim = float(np.sqrt(6.0 / (shape[0] + shape[1])))
            return jax.random.uniform(key, shape, jnp.float32, -lim, lim)

        def _gcn_norm(edge_index, edge_weight, num_nodes):
            loops = jnp.arange(num_nodes, dtype=edge_index.dtype)
            row = jnp.concatenate([edge_index[0], loops])
            col = jnp.concatenate([edge_index[1], loops])
            w = jnp.concatenate([edge_weight, jnp.ones((num_nodes,), edge_weight.dtype)])
            deg = jax.ops.segment_sum(w, col, num_segments=num_nodes)
            dinv = jnp.where(deg > 0, jax.lax.rsqrt(deg), 0.0)
            norm = dinv[row] * w * dinv[col]
            return (row, col, norm)

        def _gcn_conv(x, row, col, norm, W, b):
            h = x @ W
            msg = norm[:, None] * h[row]
            out = jax.ops.segment_sum(msg, col, num_segments=x.shape[0])
            return out + b
        key = jax.random.key(seed)
        ks = jax.random.split(key, 9)
        x = jax.random.normal(ks[0], (N_NODES, IN_F), jnp.float32)
        edge_index = jax.random.randint(ks[1], (2, N_EDGES), 0, N_NODES, jnp.int64)
        edge_weight = jax.random.uniform(ks[2], (N_EDGES,), jnp.float32)
        W0 = _glorot(ks[3], (IN_F, HID))
        b0 = jnp.zeros((HID,), jnp.float32)
        W1 = _glorot(ks[4], (HID, HID))
        b1 = jnp.zeros((HID,), jnp.float32)
        W2 = _glorot(ks[5], (HID, N_CLASSES))
        b2 = jnp.zeros((N_CLASSES,), jnp.float32)
        return {'x': x, 'edge_index': edge_index, 'edge_weight': edge_weight, 'W0': W0, 'b0': b0, 'W1': W1, 'b1': b1, 'W2': W2, 'b2': b2}
    _L0_gnn_all = _L0_gnn_setup()
    _L0_gnn_in = {k: v for k, v in _L0_gnn_all.items() if k in ('W0', 'b0', 'W1', 'b1', 'W2', 'b2')}
    del _L0_gnn_all

    def _L1_gnn_setup():
        import jax, jax.numpy as jnp
        import numpy as np
        N_NODES = 50000
        N_EDGES = 25000
        D_FEAT = 128
        UNITS = 128
        key = jax.random.key(seed)
        k1, k2, k3, k4, k5 = jax.random.split(key, 5)
        node_states = jax.random.normal(k1, (N_NODES, D_FEAT), dtype=jnp.float32)
        src = jnp.sort(jax.random.randint(k2, (N_EDGES,), 0, N_NODES))
        dst = jax.random.randint(k3, (N_EDGES,), 0, N_NODES)
        edges = jnp.stack([src, dst], axis=1).astype(jnp.int64)
        kernel = jax.random.normal(k4, (D_FEAT, UNITS), dtype=jnp.float32) * (1.0 / np.sqrt(D_FEAT))
        kernel_attention = jax.random.normal(k5, (2 * UNITS, 1), dtype=jnp.float32) * (1.0 / np.sqrt(2 * UNITS))
        return {'node_states': node_states, 'edges': edges, 'kernel': kernel, 'kernel_attention': kernel_attention}
    _L1_gnn_all = _L1_gnn_setup()
    _L1_gnn_in = {k: v for k, v in _L1_gnn_all.items() if k in ('kernel', 'kernel_attention')}
    del _L1_gnn_all

    def _L2_gnn_setup():
        import jax, jax.numpy as jnp
        import numpy as np
        N_NODES = 50000
        N_EDGES = 25000
        D_MODEL = 128
        N_HEADS = 8
        D_HEAD = D_MODEL // N_HEADS
        EPS_BN = 1e-05

        def _batchnorm(h, g, b):
            mu = jnp.mean(h, axis=0, keepdims=True)
            var = jnp.var(h, axis=0, keepdims=True)
            return (h - mu) * jax.lax.rsqrt(var + EPS_BN) * g + b
        key = jax.random.key(seed)
        ks = jax.random.split(key, 16)
        s = 0.05
        inp = {'x': jax.random.normal(ks[0], (N_NODES, D_MODEL), jnp.float32), 'edge_attr': jax.random.normal(ks[1], (N_EDGES, 1), jnp.float32), 'edge_index': jax.random.randint(ks[2], (2, N_EDGES), 0, N_NODES, jnp.int32), 'Wq': jax.random.normal(ks[3], (D_MODEL, D_MODEL), jnp.float32) * s, 'Wk': jax.random.normal(ks[4], (D_MODEL, D_MODEL), jnp.float32) * s, 'We': jax.random.normal(ks[5], (1, D_MODEL), jnp.float32) * s, 'Wv': jax.random.normal(ks[6], (D_MODEL, D_MODEL), jnp.float32) * s, 'Wo': jax.random.normal(ks[7], (D_MODEL, D_MODEL), jnp.float32) * s, 'bo': jnp.zeros((D_MODEL,), jnp.float32), 'g1': jnp.ones((D_MODEL,), jnp.float32), 'b1': jnp.zeros((D_MODEL,), jnp.float32), 'W1': jax.random.normal(ks[8], (D_MODEL, 2 * D_MODEL), jnp.float32) * s, 'bf1': jnp.zeros((2 * D_MODEL,), jnp.float32), 'W2': jax.random.normal(ks[9], (2 * D_MODEL, D_MODEL), jnp.float32) * s, 'bf2': jnp.zeros((D_MODEL,), jnp.float32), 'g2': jnp.ones((D_MODEL,), jnp.float32), 'b2': jnp.zeros((D_MODEL,), jnp.float32)}
        return inp
    _L2_gnn_all = _L2_gnn_setup()
    _L2_gnn_in = {k: v for k, v in _L2_gnn_all.items() if k in ('Wq', 'Wk', 'We', 'Wv', 'Wo', 'bo', 'g1', 'b1', 'W1', 'bf1', 'W2', 'bf2', 'g2', 'b2')}
    del _L2_gnn_all

    def _L3_gnn_setup():
        import jax, jax.numpy as jnp
        import numpy as np
        N_NODES = 50000
        N_EDGES = 18750
        D_FEAT = 128
        key = jax.random.key(seed)
        k_h, k_src, k_dst, k_dt, k_norm = jax.random.split(key, 5)
        h = jax.random.normal(k_h, (N_NODES, D_FEAT), dtype=jnp.float32)
        src = jax.random.randint(k_src, (N_EDGES,), 0, N_NODES, dtype=jnp.int32)
        dst = jax.random.randint(k_dst, (N_EDGES,), 0, N_NODES, dtype=jnp.int32)
        dt = jax.random.uniform(k_dt, (N_EDGES,), dtype=jnp.float32) * 10.0
        norm = jax.random.uniform(k_norm, (N_EDGES,), dtype=jnp.float32)
        decay_lam = jnp.full((1,), 0.1, dtype=jnp.float32)
        return {'h': h, 'src': src, 'dst': dst, 'dt': dt, 'norm': norm, 'decay_lam': decay_lam}
    _L3_gnn_all = _L3_gnn_setup()
    _L3_gnn_in = {k: v for k, v in _L3_gnn_all.items() if k in ('decay_lam',)}
    del _L3_gnn_all
    return {'x': x, 'src': src, 'dst': dst, 'edge_weight': edge_weight, 'edge_weight_n2': edge_weight_n2, 'edge_weight1': edge_weight1, 'L0_gnn_W0': _L0_gnn_in['W0'], 'L0_gnn_b0': _L0_gnn_in['b0'], 'L0_gnn_W1': _L0_gnn_in['W1'], 'L0_gnn_b1': _L0_gnn_in['b1'], 'L0_gnn_W2': _L0_gnn_in['W2'], 'L0_gnn_b2': _L0_gnn_in['b2'], 'L1_gnn_kernel': _L1_gnn_in['kernel'], 'L1_gnn_kernel_attention': _L1_gnn_in['kernel_attention'], 'L2_gnn_Wq': _L2_gnn_in['Wq'], 'L2_gnn_Wk': _L2_gnn_in['Wk'], 'L2_gnn_We': _L2_gnn_in['We'], 'L2_gnn_Wv': _L2_gnn_in['Wv'], 'L2_gnn_Wo': _L2_gnn_in['Wo'], 'L2_gnn_bo': _L2_gnn_in['bo'], 'L2_gnn_g1': _L2_gnn_in['g1'], 'L2_gnn_b1': _L2_gnn_in['b1'], 'L2_gnn_W1': _L2_gnn_in['W1'], 'L2_gnn_bf1': _L2_gnn_in['bf1'], 'L2_gnn_W2': _L2_gnn_in['W2'], 'L2_gnn_bf2': _L2_gnn_in['bf2'], 'L2_gnn_g2': _L2_gnn_in['g2'], 'L2_gnn_b2': _L2_gnn_in['b2'], 'L3_gnn_decay_lam': _L3_gnn_in['decay_lam']}

def reference(x, src, dst, edge_weight, edge_weight_n2, edge_weight1, L0_gnn_W0, L0_gnn_b0, L0_gnn_W1, L0_gnn_b1, L0_gnn_W2, L0_gnn_b2, L1_gnn_kernel, L1_gnn_kernel_attention, L2_gnn_Wq, L2_gnn_Wk, L2_gnn_We, L2_gnn_Wv, L2_gnn_Wo, L2_gnn_bo, L2_gnn_g1, L2_gnn_b1, L2_gnn_W1, L2_gnn_bf1, L2_gnn_W2, L2_gnn_bf2, L2_gnn_g2, L2_gnn_b2, L3_gnn_decay_lam):
    import jax
    import jax.numpy as jnp

    def _L0_gnn_ref(x, edge_index, edge_weight, W0, b0, W1, b1, W2, b2):
        import jax, jax.numpy as jnp
        import numpy as np
        N_NODES = 50000
        N_EDGES = 50000
        IN_F = 128
        HID = 128
        N_CLASSES = 128

        def _glorot(key, shape):
            lim = float(np.sqrt(6.0 / (shape[0] + shape[1])))
            return jax.random.uniform(key, shape, jnp.float32, -lim, lim)

        def _gcn_norm(edge_index, edge_weight, num_nodes):
            loops = jnp.arange(num_nodes, dtype=edge_index.dtype)
            row = jnp.concatenate([edge_index[0], loops])
            col = jnp.concatenate([edge_index[1], loops])
            w = jnp.concatenate([edge_weight, jnp.ones((num_nodes,), edge_weight.dtype)])
            deg = jax.ops.segment_sum(w, col, num_segments=num_nodes)
            dinv = jnp.where(deg > 0, jax.lax.rsqrt(deg), 0.0)
            norm = dinv[row] * w * dinv[col]
            return (row, col, norm)

        def _gcn_conv(x, row, col, norm, W, b):
            h = x @ W
            msg = norm[:, None] * h[row]
            out = jax.ops.segment_sum(msg, col, num_segments=x.shape[0])
            return out + b
        n = x.shape[0]
        row, col, norm = _gcn_norm(edge_index, edge_weight, n)
        h = jax.nn.relu(_gcn_conv(x, row, col, norm, W0, b0))
        h = jax.nn.relu(_gcn_conv(h, row, col, norm, W1, b1))
        return _gcn_conv(h, row, col, norm, W2, b2)

    def _L1_gnn_ref(node_states, edges, kernel, kernel_attention):
        import jax, jax.numpy as jnp
        import numpy as np
        N_NODES = 50000
        N_EDGES = 25000
        D_FEAT = 128
        UNITS = 128
        n_nodes = node_states.shape[0]
        src, dst = (edges[:, 0], edges[:, 1])
        h = node_states @ kernel
        e_feat = jnp.concatenate([h[src], h[dst]], axis=-1)
        logits = jax.nn.leaky_relu((e_feat @ kernel_attention)[:, 0], negative_slope=0.2)
        scores = jnp.exp(jnp.clip(logits, -2.0, 2.0))
        denom = jax.ops.segment_sum(scores, src, num_segments=n_nodes)
        alpha = scores / denom[src]
        out = jax.ops.segment_sum(h[dst] * alpha[:, None], src, num_segments=n_nodes)
        return out

    def _L2_gnn_ref(x, edge_attr, edge_index, Wq, Wk, We, Wv, Wo, bo, g1, b1, W1, bf1, W2, bf2, g2, b2):
        import jax, jax.numpy as jnp
        import numpy as np
        N_NODES = 50000
        N_EDGES = 25000
        D_MODEL = 128
        N_HEADS = 8
        D_HEAD = D_MODEL // N_HEADS
        EPS_BN = 1e-05

        def _batchnorm(h, g, b):
            mu = jnp.mean(h, axis=0, keepdims=True)
            var = jnp.var(h, axis=0, keepdims=True)
            return (h - mu) * jax.lax.rsqrt(var + EPS_BN) * g + b
        N = x.shape[0]
        Q = (x @ Wq).reshape(N, N_HEADS, D_HEAD)
        K = (x @ Wk).reshape(N, N_HEADS, D_HEAD)
        V = (x @ Wv).reshape(N, N_HEADS, D_HEAD)
        E = (edge_attr @ We).reshape(-1, N_HEADS, D_HEAD)
        src_idx = edge_index[0]
        dst_idx = edge_index[1]
        score = K[src_idx] * Q[dst_idx] * (1.0 / np.sqrt(D_HEAD)) * E
        score = jnp.exp(jnp.clip(jnp.sum(score, axis=-1, keepdims=True), -5.0, 5.0))
        msg = V[src_idx] * score
        wV = jax.ops.segment_sum(msg, dst_idx, num_segments=N)
        Z = jax.ops.segment_sum(score, dst_idx, num_segments=N)
        h_attn = (wV / (Z + 1e-06)).reshape(N, D_MODEL)
        h = h_attn @ Wo + bo
        h = x + h
        h = _batchnorm(h, g1, b1)
        h_in2 = h
        h = jax.nn.relu(h @ W1 + bf1)
        h = h @ W2 + bf2
        h = h_in2 + h
        h = _batchnorm(h, g2, b2)
        return h

    def _L3_gnn_ref(h, src, dst, dt, norm, decay_lam):
        import jax, jax.numpy as jnp
        import numpy as np
        N_NODES = 50000
        N_EDGES = 18750
        D_FEAT = 128
        lam = jax.nn.relu(decay_lam[0]) + 0.0001
        w = norm * jnp.exp(-lam * dt)
        m = h[src] * w[:, None]
        h_new = jax.ops.segment_sum(m, dst, num_segments=h.shape[0])
        return h_new
    edge_index = jnp.stack([src, dst])
    edge_index_t = jnp.stack([src, dst], axis=1)
    h = jnp.maximum(_layernorm(x, axis=-1), 0.0)
    x = x + _L0_gnn_ref(h, edge_index, edge_weight, L0_gnn_W0, L0_gnn_b0, L0_gnn_W1, L0_gnn_b1, L0_gnn_W2, L0_gnn_b2)
    h = jnp.maximum(_layernorm(x, axis=-1), 0.0)
    x = x + _L1_gnn_ref(h, edge_index_t, L1_gnn_kernel, L1_gnn_kernel_attention)
    h = jnp.maximum(_layernorm(x, axis=-1), 0.0)
    x = x + _L2_gnn_ref(h, edge_weight1, edge_index, L2_gnn_Wq, L2_gnn_Wk, L2_gnn_We, L2_gnn_Wv, L2_gnn_Wo, L2_gnn_bo, L2_gnn_g1, L2_gnn_b1, L2_gnn_W1, L2_gnn_bf1, L2_gnn_W2, L2_gnn_bf2, L2_gnn_g2, L2_gnn_b2)
    h = jnp.maximum(_layernorm(x, axis=-1), 0.0)
    x = x + _L3_gnn_ref(h, src, dst, edge_weight, edge_weight_n2, L3_gnn_decay_lam)
    return x

_drawn_inputs = setup_inputs


def setup_inputs(seed=0):
    import zlib

    import numpy as np

    out = dict(_drawn_inputs(seed))
    spreads = {'L0_gnn_b0': (0.0, 0.268),
     'L0_gnn_b1': (0.0, 0.1),
     'L0_gnn_b2': (0.0, 0.1),
     'L2_gnn_bo': (0.0, 0.8),
     'L2_gnn_g1': (1.0, 0.6),
     'L2_gnn_b1': (0.0, 0.8),
     'L2_gnn_bf1': (0.0, 0.8),
     'L2_gnn_bf2': (0.0, 0.8),
     'L2_gnn_g2': (1.0, 0.2),
     'L2_gnn_b2': (0.0, 0.1)}
    factors = {'edge_weight': 5.069,
     'edge_weight1': 8.0,
     'L1_gnn_kernel_attention': 2.934,
     'L2_gnn_Wq': 8.0,
     'L2_gnn_Wk': 8.0,
     'L2_gnn_We': 8.0,
     'L2_gnn_Wv': 4.251,
     'L2_gnn_Wo': 4.261}
    for name, (base, spread) in spreads.items():
        noise = np.random.default_rng([zlib.crc32(name.encode()), seed]).standard_normal(out[name].shape)
        drawn = base * np.exp(spread * noise) if base else spread * noise
        out[name] = jnp.asarray(drawn.astype(out[name].dtype))
    for name, factor in factors.items():
        out[name] = (out[name] * factor).astype(out[name].dtype)
    return out
```

```python
import math
from contextlib import ExitStack

import concourse.bass as bass
from concourse import mybir

F32 = mybir.dt.float32
BF16 = mybir.dt.bfloat16
FP16 = mybir.dt.float16
I32 = mybir.dt.int32
ALU = mybir.AluOpType
ACT = mybir.ActivationFunctionType
AX_X = mybir.AxisListType.X

P = 128
N = 3125
D = 128
E = 100000
NB = -(-N // P)
NP = NB * P
TILES = 8
LANES = 125
NG = E // (TILES * LANES)
W = 64
LAST = NP - W
MAX_ROUNDS = -(-N // W) + 1
CH = 400
NC = NP // CH
SRC_CH = 640
NSC = NP // SRC_CH
SBLK = SRC_CH // P
HALF = SRC_CH // 2
NPAIR = NG // 2
STEP = 10
NSTEP = NG // STEP
HEADS = 8
DH = D // HEADS
EPS = 1e-5
E_MAX, E_MIN = math.exp(2.0), math.exp(-2.0)


def gnn(nc, x, src, dst, edge_weight, edge_weight_n2, edge_weight1, W0, b0, W1, b1, W2, b2, k1, ka,
        Wq, Wk, We, Wv, Wo, bo, g1, bb1, F1, bf1, F2, bf2, g2, bb2, decay_lam, out):
    ctx = ExitStack()

    def sb(name, shape, dt=F32):
        return ctx.enter_context(nc.sbuf_tensor(name, shape, dt))

    live = []

    def sem(name):
        live.append(nc.alloc_semaphore(name=name))
        return live[-1]

    def retire():
        nc.clear_and_free_semaphores(live)
        nc.all_engine_barrier()
        live.clear()

    def pair(name):
        return [sem(f"{name}{k}") for k in range(2)]

    def dram(name, shape, dt=F32):
        return nc.dram_tensor(name, shape, dt, kind="Internal").ap()

    with ctx:
        t_l0 = [dram(f"rows_l0_{i}", [NP, D]) for i in range(3)]
        t_l1 = dram("rows_l1", [NP, D + 2])
        t_q = dram("rows_q", [NP, D])
        t_kv = dram("rows_kv", [NP, 2 * D])
        t_l3 = dram("rows_l3", [NP, D])
        counts = dram("counts", [NPAIR, P, NP], FP16)

        XT = sb("xT", [P, NP])
        HT = sb("hT", [P, NP])
        ACC = sb("accT", [P, NP])
        ACC2 = sb("acc2T", [P, NP])
        TMP = sb("tmpT", [P, NP])
        DINV = sb("dinv_bcast", [P, NP])
        A1B = DINV
        ROWS = sb("rows", [P, NB, D + 2])

        srcI = sb("src_i", [P, NG, TILES], I32)
        srcF = sb("src_f", [P, NG, TILES])
        rel = sb("dst_rel", [P, NG, TILES])
        relc = sb("dst_rel_round", [P, NG, TILES])
        wgt = sb("edge_w", [P, NG, TILES])
        wgt3 = sb("edge_w3", [P, NG, TILES])
        attr = sb("edge_attr", [P, NG, TILES])
        base0 = sb("base0", [1, NG])
        basef = sb("base_f", [1, NG])
        basei = sb("base_i", [1, NG], I32)
        rounds_i = sb("rounds_i", [1, 2], I32)

        ident = sb("ident", [P, P])
        mean_w = sb("mean_w", [P, P])
        ones = sb("ones", [P, P])
        iota64 = sb("iota64", [P, W])
        iotaS = sb("iotaS", [P, SRC_CH], FP16)
        epst = sb("epst", [P, 1])
        lam = sb("lam", [P, 1])
        wts = sb("wts", [P, 8, D])
        wW = [wts[:, i, :] for i in range(3)]
        wk1, wq, wo = wts[:, 3, :], wts[:, 4, :], wts[:, 5, :]
        wkv = wts[:, 6:8, :]
        weB = sb("we_b", [P, D])
        f1 = sb("f1", [P, 2 * D])
        f2 = sb("f2", [P, 2, D])
        kaT = sb("ka", [P, 2])
        ka1B = sb("ka1B", [P, P])
        vec = sb("vec", [P, 11])
        B0, BO, G1, BB1, BF1, BF2, G2, BB2 = 0, 3, 4, 5, 6, 8, 9, 10
        stat = sb("stat", [P, 8])

        WORK = sb("work", [P, 6144])
        BIG = sb("big", [P, 2 * 16 * SRC_CH // 2])
        G1KV = BIG[:, 0:4 * TILES * 2 * D].rearrange("p (k t d) -> p k t d", k=4, t=TILES)
        GROW = ACC2[:, 0:2 * TILES * D].rearrange("p (k t d) -> p k t d", k=2, t=TILES)
        CB = WORK[:, 0:SRC_CH].bitcast(FP16).rearrange("p (k s) -> p k s", k=2)
        OHS = BIG[:, :].bitcast(BF16).rearrange("p (k t s) -> p k t s", k=2, t=16)
        rowst = BIG[:, 0:6 * 1000].rearrange("p (a e) -> p a e", a=6)
        OH = sb("onehot", [P, 4, TILES, W])
        idx = sb("idx", [P, 4, TILES], I32)
        OHD = sb("onehot_dst", [P, 2, 16, P], BF16)
        hwin = sb("hwin", [P, 2, D + 2])
        st_src = sb("st_src", [P, 2, 16])
        st_rel = sb("st_rel", [P, 2, 16])
        st_a2 = sb("st_a2", [P, 2])
        E1 = WORK[:, 0:1280].rearrange("p (k s) -> p k s", k=2)
        E2 = WORK[:, 1280:2560].rearrange("p (k s) -> p k s", k=2)
        SM = WORK[:, 3840:5120].rearrange("p (k s) -> p k s", k=2)
        OACC = ROWS
        OHT = WORK[:, 0:1024].rearrange("p (q t e) -> p q t e", q=2, t=4)
        QW = OHD[:, :, :, :].rearrange("p s t d -> p (s t d)").bitcast(F32)[:, 0:8 * D].rearrange("p (k d) -> p k d", k=4)
        PR = WORK[:, 1024:2048].rearrange("p (t d) -> p t d", t=TILES)
        SX = WORK[:, 2048:4096].rearrange("p (q s) -> p q s", q=2)
        MSG = WORK[:, 4096:6144].rearrange("p (q s) -> p q s", q=2)
        SC = sb("scores", [P, 2, 3, TILES * HEADS])

        big_ps = ctx.enter_context(nc.psum_tensor("psum", [P, 8, 512], F32))
        ps = [big_ps[:, i, :] for i in range(8)]
        C_PS = [big_ps[:, 2 * q:2 * q + 2, :] for q in range(2)]
        CNT_PS = [big_ps[:, 4 + 2 * q:6 + 2 * q, :] for q in range(2)]
        O_PS = [big_ps[:, 4 + 2 * q:6 + 2 * q, :] for q in range(2)]

        def ahead(eng, *sems):
            for s in sems:
                eng.sem_inc(s, 1)

        def reg_rounds(eng):
            return eng.value_load(rounds_i[0:1, 0:1], min_val=1, max_val=MAX_ROUNDS)

        loaded = sem("edges_loaded")
        x_loaded = sem("x_loaded")
        w_loaded = [sem(f"w_loaded{i}") for i in range(2)]
        consts = sem("constants_ready")
        cleared = sem("buffers_cleared")
        prep = sem("edge_rows_ready")
        e_exp = sem("decay_ready")
        e_tr = sem("edges_transposed")
        e_cp = sem("edges_copied")
        x_tr = sem("x_transposed")
        x_cp = sem("x_copied")
        b_tr = sem("bases_transposed")
        b_cp = sem("bases_ready")
        wx = sem("weights_scaled")

        srcrow = rowst[0:NG, 0, :].bitcast(I32)
        dstrow = rowst[0:NG, 1, :].bitcast(I32)
        fr = BIG[:, 6000:10000].rearrange("p (a e) -> p a e", a=4)
        r_src, r_dst, r_w3 = fr[0:NG, 0, :], fr[0:NG, 1, :], fr[0:NG, 2, :]
        r_w, r_w2, r_at = rowst[0:NG, 2, :], rowst[0:NG, 3, :], rowst[0:NG, 4, :]
        b2c = WORK[0:NG, 6000:6002]

        with nc.Block() as block:
            @block.sync
            def _(sp):
                v = lambda a: a.rearrange("(g e) -> g e", g=NG)
                sp.dma_start(dstrow, v(dst)).then_inc(loaded, 16)
                sp.dma_start(srcrow, v(src)).then_inc(loaded, 16)
                sp.dma_start(r_w, v(edge_weight)).then_inc(loaded, 16)
                sp.dma_start(r_w2, v(edge_weight_n2)).then_inc(loaded, 16)
                sp.dma_start(r_at, edge_weight1.rearrange("(g e) c -> g (e c)", g=NG)).then_inc(loaded, 16)
                sp.wait_ge(cleared, 1)
                for a, z in ((0, NB // 2), (NB // 2, NB - 1)):
                    sp.dma_start(ROWS[:, a:z, 0:D],
                                 x[a * P:z * P, :].rearrange("(b p) d -> p b d", p=P)).then_inc(x_loaded, 16)
                sp.dma_start(ROWS[0:N - (NB - 1) * P, NB - 1, 0:D], x[(NB - 1) * P:N, :]).then_inc(x_loaded, 16)
                ws = [W0, W1, W2, k1, Wq, Wo, Wk, Wv]
                for i, w_ in enumerate(ws):
                    sp.dma_start(wts[:, i, :], w_).then_inc(w_loaded[0], 16)
                sp.dma_start(weB[:, :], We.to_broadcast([P, D])).then_inc(w_loaded[0], 16)
                sp.dma_start(f1[:, :], F1).then_inc(w_loaded[0], 16)
                sp.dma_start(f2[:, :, :], F2.rearrange("(a p) d -> p a d", p=P)).then_inc(w_loaded[0], 16)

            @block.scalar
            def _(act):
                with nc.allow_non_contiguous_dma(reason="vectors of one value a partition"):
                    act.dma_start(lam[:, :], decay_lam.rearrange("(a b) -> a b", a=1).to_broadcast([P, 1])).then_inc(w_loaded[1], 16)
                    act.dma_start(kaT[:, :], ka.rearrange("(c p) o -> p (c o)", p=P)).then_inc(w_loaded[1], 16)
                    vs = [b0, b1, b2, bo, g1, bb1, bf1[0:P], bf1[P:2 * P], bf2, g2, bb2]
                    for i, v_ in enumerate(vs):
                        act.dma_start(vec[:, i:i + 1], v_.rearrange("(p o) -> p o", o=1)).then_inc(w_loaded[1], 16)
                act.wait_ge(prep, 5)
                nc.scalar.activation(r_w3, r_w, ACT.Exp, scale=lam[0:NG, :]).then_inc(e_exp, 1)
                for b in range(0, NB, 4):
                    m = min(4, NB - b)
                    act.wait_ge(x_tr, b // 4 + 1)
                    nc.scalar.copy(XT[:, b * P:(b + m) * P], ps[4 + (b // 4) % 4][:, 0:m * P]).then_inc(x_cp, 1)

            @block.gpsimd
            def _(pool):
                nc.gpsimd.memset(ROWS[:, NB - 1, :], 0.0).then_inc(cleared, 1)
                nc.gpsimd.memset(ident[:], 0.0).then_inc(consts, 1)
                pool.wait_ge(consts, 1)
                nc.gpsimd.affine_select(out=ident[:], in_=ident[:], compare_op=ALU.not_equal, fill=1.0, base=0,
                                        pattern=[[-1, P]], channel_multiplier=1).then_inc(consts, 1)
                nc.gpsimd.iota(iota64[:], [[1, W]], base=0, channel_multiplier=0,
                               allow_small_or_imprecise_dtypes=True).then_inc(consts, 1)
                nc.gpsimd.iota(iotaS[:], [[1, SRC_CH]], base=0, channel_multiplier=0,
                               allow_small_or_imprecise_dtypes=True).then_inc(consts, 1)
                for t, v in ((rel, float(E)), (srcF, 0.0), (wgt, 0.0), (wgt3, 0.0), (attr, 0.0)):
                    nc.gpsimd.memset(t[:], v).then_inc(cleared, 1)
                for t, v in ((mean_w, 1.0 / D), (ones, 1.0), (epst, EPS), (OHD, 0.0)):
                    nc.gpsimd.memset(t[:], v).then_inc(cleared, 1)

            @block.vector
            def _(dve):
                dve.wait_ge(loaded, 16 * 5)
                nc.vector.tensor_copy(r_dst, dstrow).then_inc(prep, 1)
                nc.vector.tensor_copy(r_src, srcrow).then_inc(prep, 1)
                dve.wait_ge(w_loaded[1], 16 * 13)
                nc.vector.tensor_scalar(lam[:], lam[:], 0.0, 1e-4, ALU.max, ALU.add).then_inc(prep, 1)
                dve.wait_ge(prep, 3)
                nc.vector.tensor_scalar(lam[:], lam[:], -1.0, None, ALU.mult).then_inc(prep, 1)
                nc.vector.tensor_reduce(b2c[:, 0:1], r_dst, AX_X, ALU.min).then_inc(prep, 1)
                nc.vector.tensor_reduce(b2c[:, 1:2], r_dst, AX_X, ALU.max).then_inc(prep, 1)
                dve.wait_ge(prep, 6)
                nc.vector.tensor_scalar(r_dst, r_dst, b2c[:, 0:1], None, ALU.subtract).then_inc(prep, 1)
                dve.wait_ge(e_exp, 1)
                nc.vector.tensor_tensor(r_w3, r_w3, r_w2, ALU.mult).then_inc(prep, 1)
                dve.wait_ge(cleared, 6)
                cp = 0
                for a, t in enumerate((rel, srcF, wgt, wgt3, attr)):
                    for h in range(2):
                        dve.wait_ge(e_tr, cp + 1)
                        nc.vector.tensor_copy(t[0:LANES, :, 4 * h:4 * h + 4].rearrange("p g t -> p t g"),
                                              ps[cp % 4][0:LANES, 0:4 * NG].rearrange("p (t g) -> p t g", t=4)).then_inc(e_cp, 1)
                        cp += 1
                dve.wait_ge(b_tr, 1)
                nc.vector.tensor_copy(base0[:], ps[0][0:1, 0:NG]).then_inc(b_cp, 1)
                nc.vector.tensor_copy(basef[:], ps[0][0:1, P:P + NG]).then_inc(b_cp, 1)
                dve.wait_ge(b_cp, 2)
                nc.vector.tensor_tensor(basef[:], basef[:], base0[:], ALU.subtract).then_inc(b_cp, 1)
                dve.wait_ge(b_cp, 3)
                nc.vector.tensor_reduce(stat[0:1, 0:1], basef[:], AX_X, ALU.max).then_inc(b_cp, 1)
                dve.wait_ge(b_cp, 4)
                nc.vector.tensor_copy(rounds_i[:, 1:2], stat[0:1, 0:1]).then_inc(b_cp, 1)
                dve.wait_ge(b_cp, 5)
                nc.vector.tensor_scalar(rounds_i[:, 1:2], rounds_i[:, 1:2], 6, None, ALU.arith_shift_right).then_inc(b_cp, 1)
                dve.wait_ge(b_cp, 6)
                nc.vector.tensor_scalar(rounds_i[:, 0:1], rounds_i[:, 1:2], 1, None, ALU.add).then_inc(b_cp, 1)
                dve.wait_ge(e_cp, 10)
                nc.vector.tensor_copy(srcI[:], srcF[:]).then_inc(b_cp, 1)
                dve.wait_ge(w_loaded[0], 16 * 11)
                nc.vector.tensor_scalar(weB[:], weB[:], 1.0 / DH ** 0.5, None, ALU.mult).then_inc(wx, 1)
                dve.wait_ge(wx, 1)
                nc.vector.tensor_tensor(wkv[:, 0, :], wkv[:, 0, :], weB[:], ALU.mult).then_inc(wx, 1)
                dve.wait_ge(cleared, 9)
                nc.vector.tensor_scalar(ka1B[:], ones[:], kaT[:, 0:1], None, ALU.mult).then_inc(wx, 1)
                dve.wait_ge(wx, 3)
                dve.wait_ge(b_cp, 8)

            @block.tensor
            def _(pe):
                pe.wait_ge(consts, 2)
                pe.wait_ge(prep, 8)
                cp = 0
                for r in (r_dst, r_src, r_w, r_w3, r_at):
                    for h in range(2):
                        if cp >= 4:
                            pe.wait_ge(e_cp, cp - 3)
                        for t in range(4):
                            last = nc.tensor.transpose(ps[cp % 4][0:LANES, t * NG:(t + 1) * NG],
                                                       r[:, (4 * h + t) * LANES:(4 * h + t + 1) * LANES],
                                                       ident[0:NG, 0:NG])
                        last.then_inc(e_tr, 1)
                        cp += 1
                pe.wait_ge(e_cp, 10)
                nc.tensor.transpose(ps[0][0:1, 0:NG], b2c[:, 0:1], ident[0:NG, 0:NG])
                nc.tensor.transpose(ps[0][0:1, P:P + NG], b2c[:, 1:2], ident[0:NG, 0:NG]).then_inc(b_tr, 1)
                pe.wait_ge(x_loaded, 48)
                pe.wait_ge(cleared, 1)
                for b in range(0, NB, 4):
                    if b // 4 >= 4:
                        pe.wait_ge(x_cp, b // 4 - 3)
                    for j in range(min(4, NB - b)):
                        last = nc.tensor.transpose(ps[4 + (b // 4) % 4][:, j * P:(j + 1) * P], ROWS[:, b + j, 0:D], ident[:])
                    last.then_inc(x_tr, 1)

        retire()

        def chunk(t, c):
            return t[:, c * CH:(c + 1) * CH]

        def layer_norm(name):
            mean, cent, sq, var, std, inv, done = (sem(f"{name}_{s}") for s in
                                                   ("mean", "centred", "squared", "var", "std", "inv", "normed"))
            with nc.Block() as block:
                @block.tensor
                def _(pe):
                    for c in range(NC):
                        nc.tensor.matmul(ps[c][:, 0:CH], mean_w[:], chunk(XT, c), start=True, stop=True).then_inc(mean, 1)
                    for c in range(NC):
                        pe.wait_ge(sq, c + 1)
                        nc.tensor.matmul(ps[c][:, 0:CH], mean_w[:], chunk(TMP, c), start=True, stop=True).then_inc(var, 1)

                @block.vector
                def _(dve):
                    for c in range(NC):
                        dve.wait_ge(mean, c + 1)
                        nc.vector.tensor_tensor(chunk(HT, c), chunk(XT, c), ps[c][:, 0:CH], ALU.subtract).then_inc(cent, 1)
                    for c in range(NC):
                        dve.wait_ge(std, c + 1)
                        nc.vector.reciprocal(chunk(TMP, c), chunk(TMP, c)).then_inc(inv, 1)
                        dve.wait_ge(inv, c + 1)
                        nc.vector.scalar_tensor_tensor(out=chunk(HT, c), in0=chunk(HT, c), scalar=0.0, in1=chunk(TMP, c),
                                                       op0=ALU.max, op1=ALU.mult).then_inc(done, 1)

                @block.scalar
                def _(act):
                    for c in range(NC):
                        act.wait_ge(cent, c + 1)
                        nc.scalar.activation(chunk(TMP, c), chunk(HT, c), ACT.Square).then_inc(sq, 1)
                    for c in range(NC):
                        act.wait_ge(var, c + 1)
                        nc.scalar.activation(chunk(TMP, c), ps[c][:, 0:CH], ACT.Sqrt, bias=epst[:]).then_inc(std, 1)

        def project(name, outT, weight, inT):
            mm, cp = sem(f"{name}_projected"), sem(f"{name}_copied")
            with nc.Block() as block:
                @block.tensor
                def _(pe):
                    for c in range(NC):
                        nc.tensor.matmul(ps[c][:, 0:CH], weight, chunk(inT, c), start=True, stop=True).then_inc(mm, 1)

                @block.vector
                def _(dve):
                    for c in range(0, NC, 2):
                        dve.wait_ge(mm, c + 1)
                        nc.vector.tensor_copy(chunk(outT, c), ps[c][:, 0:CH]).then_inc(cp, 1)

                @block.scalar
                def _(act):
                    for c in range(1, NC, 2):
                        act.wait_ge(mm, c + 1)
                        nc.scalar.copy(chunk(outT, c), ps[c][:, 0:CH]).then_inc(cp, 1)

        def store_rows(name, inT, weight, table, width=D):
            mm, cpa, cpv, st = (sem(f"{name}_{s}") for s in ("multiplied", "copied_act", "copied_dve", "stored"))
            per = 512 // width
            steps = [(b, min(per, NB - b)) for b in range(0, NB, per)]
            parts = 4 if width == D else 3
            first, second = steps[0::2], steps[1::2]
            with nc.Block() as block:
                @block.tensor
                def _(pe):
                    for i, (b, m) in enumerate(steps):
                        if i >= 8:
                            pe.wait_ge(cpa if i % 2 else cpv, (i - 8) // 2 + 1)
                        for j in range(m):
                            last = nc.tensor.matmul(ps[i % 8][:, j * width:(j + 1) * width], inT[:, (b + j) * P:(b + j + 1) * P],
                                                    weight, start=True, stop=True)
                        last.then_inc(mm, 1)

                def copies(eng, copy, done, mine, at):
                    for i, (b, m) in enumerate(mine):
                        k = 2 * i + at
                        eng.wait_ge(mm, k + 1)
                        if width == D:
                            o = ROWS[:, b:b + m, 0:D]
                            copy(o, ps[k % 8][:, 0:m * D].rearrange("p (b d) -> p b d", d=D)).then_inc(done, 1)
                        else:
                            if i >= 2:
                                eng.wait_ge(st, 16 * (k - 3))
                            o = KVR[:, k % 4, 0:m * width]
                            copy(o, ps[k % 8][:, 0:m * width]).then_inc(done, 1)

                KVR = WORK[:, 0:2048].rearrange("p (k s) -> p k s", k=4)

                @block.vector
                def _(dve):
                    copies(dve, nc.vector.tensor_copy, cpv, first, 0)

                @block.scalar
                def _(act):
                    copies(act, nc.scalar.copy, cpa, second, 1)

                @block.sync
                def _(sp):
                    tv = table.rearrange("(b p) d -> p b d", p=P)
                    if width == D:
                        sp.wait_ge(cpv, len(first))
                        sp.wait_ge(cpa, len(second))
                        sp.dma_start(tv, ROWS[:, :, 0:D]).then_inc(st, 16)
                        sp.wait_ge(st, 16)
                    else:
                        for k, (b, m) in enumerate(steps):
                            sp.wait_ge(cpa if k % 2 else cpv, k // 2 + 1)
                            if k:
                                sp.wait_ge(st, 16 * k)
                            sp.dma_start(tv[:, b:b + m, :], KVR[:, k % 4, 0:m * width].rearrange("p (b d) -> p b d", d=width)).then_inc(st, 16)
                        sp.wait_ge(st, 16 * len(steps))
            return st

        NI = NG // 2

        def round_setup(dve, sems, r):
            upd, opened = sems
            v = r * 3
            nc.vector.tensor_scalar(relc[:], relc[:], float(W), None, ALU.subtract).then_inc(upd, 1)
            nc.vector.tensor_scalar(basef[:], basef[:], float(W), float(LAST), ALU.add, ALU.min).then_inc(upd, 1)
            dve.wait_ge(upd, v + 2)
            nc.vector.tensor_copy(basei[:], basef[:]).then_inc(upd, 1)
            dve.wait_ge(upd, v + 3)
            dve.sem_inc(opened, 1)

        def round_reset(dve, reset):
            nc.vector.tensor_scalar(relc[:], rel[:], float(W), None, ALU.add).then_inc(reset, 1)
            nc.vector.tensor_scalar(basef[:], base0[:], float(W), None, ALU.subtract).then_inc(reset, 1)
            dve.wait_ge(reset, 2)

        def pair_dst_onehot(s, done):
            for h in range(2):
                nc.vector.tensor_tensor(OHD[:, s, h * TILES:(h + 1) * TILES, h * W:(h + 1) * W],
                                        iota64[:, None, :].to_broadcast([P, TILES, W]),
                                        st_rel[:, s, h * TILES:(h + 1) * TILES, None].to_broadcast([P, TILES, W]),
                                        ALU.is_equal).then_inc(done, 1)

        def aggregate(name, table, weights, acc, first_pair=None, count_steps=0):
            reset, upd, opened, go = (sem(f"{name}_{s}") for s in ("reset", "windows", "round", "gather_go"))
            s_idx, s_g, s_eq, s_oh, s_mm, s_ev = (pair(f"{name}_{s}") for s in
                                                  ("index", "gathered", "equal", "onehot", "summed", "added"))
            s_src, s_rel, s_ohd, s_osd, s_c, s_cev, s_cst, s_cfree = (
                pair(f"{name}_{s}") for s in ("src_staged", "rel_staged", "dst_onehot", "src_onehot", "counted",
                                              "counts_read", "counts_stored", "counts_free"))
            HS = STEP // 2

            def rounds(eng, R, steps, begin=lambda r: None):
                begin(0)
                if count_steps:
                    with eng.Fori(0, count_steps) as i:
                        steps(i * HS, i, True)
                if count_steps < NSTEP:
                    with eng.Fori(count_steps, NSTEP) as i:
                        steps(i * HS, i, False)
                with eng.If(R > 1):
                    with eng.Fori(1, R) as r:
                        begin(r)
                        with eng.Fori(0, NSTEP) as i:
                            steps(r * NI + i * HS, i, False)

            with nc.Block() as block:
                @block.scalar
                def _(act):
                    ahead(act, *s_cev)

                    def steps(n, i, counting):
                        def index(j):
                            k = j % 2
                            act.wait_ge(s_mm[k], n + j // 2 + 1)
                            nc.scalar.copy(idx[:, k, :], srcI[:, bass.ds(STEP * i + j, 1), :]).then_inc(s_idx[k], 1)

                        def stage(s):
                            act.wait_ge(s_c[1], n + 1)
                            g = 2 * first_pair + 4 * i + 2 * s
                            nc.scalar.copy(st_src[:, s, :].rearrange("p (g t) -> p g t", g=2), srcF[:, bass.ds(g, 2), :]).then_inc(s_src[s], 1)
                            nc.scalar.copy(st_rel[:, s, :].rearrange("p (g t) -> p g t", g=2), relc[:, bass.ds(g, 2), :]).then_inc(s_rel[s], 1)

                        def read_counts(j):
                            q = j % 2
                            act.wait_ge(s_cfree[q], n + j // 2 + 1)
                            act.wait_ge(s_c[q], n + j // 2 + 2)
                            nc.scalar.copy(CB[:, q, :].rearrange("p (h s) -> p h s", h=2), CNT_PS[q][:, :, 0:HALF]).then_inc(s_cev[q], 1)

                        if counting:
                            stage(0)
                        index(0)
                        for j in range(STEP):
                            if j + 1 < STEP:
                                index(j + 1)
                            if counting:
                                if j == 0:
                                    stage(1)
                                read_counts(j)

                    if count_steps:
                        act.wait_ge(opened, 1)
                    R = reg_rounds(act)
                    rounds(act, R, steps)

                @block.gpsimd
                def _(pool):
                    def steps(n, i, counting):
                        for j in range(STEP):
                            k = j % 2
                            pool.wait_ge(s_idx[k], n + j // 2 + 1)
                            pool.wait_ge(s_mm[k], n + j // 2 + 1)
                            pool.sem_inc(go, 1)
                            for t in range(TILES):
                                pool.indirect_dma_start(
                                    out=GROW[:, k, t, :], out_offset=None, in_=table,
                                    in_offset=bass.IndirectOffsetOnAxis(ap=idx[:, k, t:t + 1], axis=0),
                                ).then_inc(s_g[k], 16)

                    R = reg_rounds(pool)
                    rounds(pool, R, steps)

                @block.vector
                def _(dve):
                    ahead(dve, *s_ev)

                    def steps(n, i, counting):
                        def onehot(j):
                            k, u = j % 2, n + j // 2
                            g = bass.ds(STEP * i + j, 1)
                            dve.wait_ge(s_mm[k], u + 1)
                            nc.vector.tensor_tensor(
                                OH[:, k, :, :], iota64[:, None, :].to_broadcast([P, TILES, W]),
                                relc[:, g, :].rearrange("p g t -> p (g t)")[:, :, None].to_broadcast([P, TILES, W]),
                                ALU.is_equal).then_inc(s_eq[k], 1)
                            dve.wait_ge(s_eq[k], u + 1)
                            nc.vector.tensor_tensor(
                                OH[:, k, :, :], OH[:, k, :, :],
                                weights[:, g, :].rearrange("p g t -> p (g t)")[:, :, None].to_broadcast([P, TILES, W]),
                                ALU.mult).then_inc(s_oh[k], 1)

                        def add(j):
                            k, u = j % 2, n + j // 2
                            b = dve.value_load(basei[0:1, bass.ds(STEP * i + j, 1)], min_val=0, max_val=LAST)
                            dve.wait_ge(s_ev[1 - k], u + k + 1)
                            dve.wait_ge(s_mm[k], u + 2)
                            nc.vector.tensor_tensor(acc[:, bass.ds(b, W)], acc[:, bass.ds(b, W)],
                                                    ps[k][:, 0:W], ALU.add).then_inc(s_ev[k], 1)

                        def pair_onehots(j):
                            s, c, q = j // NSC, j % NSC, j % 2
                            if c == 0:
                                dve.wait_ge(s_rel[s], i + 1)
                                dve.wait_ge(s_c[1], n + 1)
                                pair_dst_onehot(s, s_ohd[s])
                                dve.wait_ge(s_src[s], i + 1)
                            dve.wait_ge(s_c[q], n + j // 2 + 1)
                            for t in range(16):
                                last = nc.vector.tensor_scalar(OHS[:, q, t, :], iotaS[:], st_src[:, s, t:t + 1], -float(c * SRC_CH),
                                                               ALU.subtract, ALU.is_equal)
                            last.then_inc(s_osd[q], 1)

                        for j in range(STEP):
                            onehot(j)
                            if counting:
                                pair_onehots(j)
                            if j:
                                add(j - 1)
                        add(STEP - 1)

                    def begin(r):
                        round_setup(dve, [upd, opened], r)

                    R = reg_rounds(dve)
                    round_reset(dve, reset)
                    rounds(dve, R, steps, begin)

                @block.tensor
                def _(pe):
                    ahead(pe, *s_mm, *s_c)

                    def steps(n, i, counting):
                        for j in range(STEP):
                            k, u = j % 2, n + j // 2
                            if counting:
                                s, c, q = j // NSC, j % NSC, j % 2
                                if c == 0:
                                    pe.wait_ge(s_ohd[s], 2 * i + 2)
                                pe.wait_ge(s_cev[q], u + 1)
                                pe.wait_ge(s_osd[q], u + 1)
                                for h in range(2):
                                    for t in range(16):
                                        last = nc.tensor.matmul(CNT_PS[q][:, h, 0:HALF], OHD[:, s, t, :],
                                                                OHS[:, q, t, h * HALF:(h + 1) * HALF], start=(t == 0), stop=(t == 15))
                                last.then_inc(s_c[q], 1)
                            pe.wait_ge(s_ev[k], u + 1)
                            pe.wait_ge(s_oh[k], u + 1)
                            pe.wait_ge(s_g[k], u * (16 * TILES) + 16 * TILES)
                            for t in range(TILES):
                                last = nc.tensor.matmul(ps[k][:, 0:W], GROW[:, k, t, :], OH[:, k, t, :],
                                                        start=(t == 0), stop=(t == TILES - 1))
                            last.then_inc(s_mm[k], 1)

                    R = reg_rounds(pe)
                    rounds(pe, R, steps)

                if count_steps:
                    @block.sync
                    def _(sp):
                        ahead(sp, *s_cfree)
                        with sp.Fori(0, count_steps) as i:
                            for j in range(STEP):
                                s, c, q = j // NSC, j % NSC, j % 2
                                u = i * HS + j // 2
                                sp.wait_ge(s_cev[q], u + 2)
                                sp.dma_start(counts[bass.ds(first_pair + 2 * i + s, 1), :, c * SRC_CH:(c + 1) * SRC_CH].rearrange("g p s -> p (g s)"),
                                             CB[:, q, :]).then_inc(s_cst[q], 16)
                                sp.wait_ge(s_cst[q], u * 16 + 16)
                                sp.sem_inc(s_cfree[q], 1)

        def degrees(acc):
            SL = 4
            NI4 = NG // SL
            reset, upd, opened = sem("deg_reset"), sem("deg_windows"), sem("deg_round")
            s_w, s_oh, s_mm, s_ev = ([sem(f"deg_{s}{k}") for k in range(SL)] for s in ("weights", "onehot", "summed", "added"))
            WS = WORK[:, 0:SL * TILES].rearrange("p (k t) -> p k t", k=SL)
            with nc.Block() as block:
                @block.scalar
                def _(act):
                    R = reg_rounds(act)
                    with act.Fori(0, R) as r:
                        with act.Fori(0, NI4) as i:
                            n = r * NI4 + i
                            for k in range(SL):
                                act.wait_ge(s_mm[k], n + 1)
                                nc.scalar.copy(WS[:, k, :], wgt[:, bass.ds(SL * i + k, 1), :]).then_inc(s_w[k], 1)

                @block.vector
                def _(dve):
                    ahead(dve, *s_ev)
                    R = reg_rounds(dve)
                    round_reset(dve, reset)
                    with dve.Fori(0, R) as r:
                        round_setup(dve, [upd, opened], r)
                        with dve.Fori(0, NI4) as i:
                            n = r * NI4 + i
                            for k in range(SL):
                                dve.wait_ge(s_mm[k], n + 1)
                                nc.vector.tensor_tensor(
                                    OH[:, k, :, :], iota64[:, None, :].to_broadcast([P, TILES, W]),
                                    relc[:, bass.ds(SL * i + k, 1), :].rearrange("p g t -> p (g t)")[:, :, None].to_broadcast([P, TILES, W]),
                                    ALU.is_equal).then_inc(s_oh[k], 1)
                            for k in range(SL):
                                b = dve.value_load(basei[0:1, bass.ds(SL * i + k, 1)], min_val=0, max_val=LAST)
                                dve.wait_ge(s_ev[(k - 1) % SL], n + 1 + (k > 0))
                                dve.wait_ge(s_mm[k], n + 2)
                                nc.vector.tensor_tensor(acc[:, bass.ds(b, W)], acc[:, bass.ds(b, W)],
                                                        ps[k][:, 0:W], ALU.add).then_inc(s_ev[k], 1)

                @block.tensor
                def _(pe):
                    ahead(pe, *s_mm)
                    R = reg_rounds(pe)
                    with pe.Fori(0, R) as r:
                        with pe.Fori(0, NI4) as i:
                            n = r * NI4 + i
                            for k in range(SL):
                                pe.wait_ge(s_ev[k], n + 1)
                                pe.wait_ge(s_w[k], n + 1)
                                pe.wait_ge(s_oh[k], n + 1)
                                for t in range(TILES):
                                    last = nc.tensor.matmul(ps[k][:, 0:W], WS[:, k, t:t + 1].to_broadcast([P, P]), OH[:, k, t, :],
                                                            start=(t == 0), stop=(t == TILES - 1))
                                last.then_inc(s_mm[k], 1)

        def on_vector(name, steps):
            s = sem(name)
            with nc.Block() as block:
                @block.vector
                def _(dve):
                    for i, step in enumerate(steps):
                        if i:
                            dve.wait_ge(s, i)
                        step().then_inc(s, 1)

        V = nc.vector

        on_vector("deg_start", [lambda: V.memset(DINV[:], 1.0)])
        degrees(DINV)
        droot, dinv = sem("deg_root"), sem("deg_inverse")
        with nc.Block() as block:
            @block.vector
            def _(dve):
                nc.vector.tensor_scalar(TMP[:], DINV[:], 0.0, None, ALU.is_gt).then_inc(dinv, 1)
                nc.vector.tensor_scalar(DINV[:], DINV[:], 1e-30, None, ALU.max).then_inc(dinv, 1)
                dve.wait_ge(droot, 1)
                nc.vector.reciprocal(DINV[:], DINV[:]).then_inc(dinv, 1)
                dve.wait_ge(dinv, 3)
                nc.vector.tensor_tensor(DINV[:], DINV[:], TMP[:], ALU.mult).then_inc(dinv, 1)

            @block.scalar
            def _(act):
                act.wait_ge(dinv, 2)
                nc.scalar.activation(DINV[:], DINV[:], ACT.Sqrt).then_inc(droot, 1)

        layer_norm("ln0")
        retire()
        for l in range(3):
            on_vector(f"l0_{l}_scale", [lambda: V.tensor_tensor(HT[:], HT[:], DINV[:], ALU.mult)])
            project(f"l0_{l}_self", ACC, wW[l], HT)
            store_rows(f"l0_{l}_rows", HT, wW[l], t_l0[l])
            aggregate(f"l0_{l}_sum", t_l0[l], wgt, ACC, 2 * NSTEP * l, min(NSTEP, (NPAIR - 2 * NSTEP * l) // 2))
            bias = vec[:, B0 + l:B0 + l + 1]
            if l < 2:
                on_vector(f"l0_{l}_end", [lambda: V.tensor_tensor(ACC[:], ACC[:], DINV[:], ALU.mult),
                                          lambda: V.tensor_scalar(HT[:], ACC[:], bias, 0.0, ALU.add, ALU.max)])
            else:
                on_vector(f"l0_{l}_end", [lambda: V.tensor_tensor(ACC[:], ACC[:], DINV[:], ALU.mult),
                                          lambda: V.scalar_tensor_tensor(out=XT[:], in0=ACC[:], scalar=bias, in1=XT[:],
                                                                         op0=ALU.add, op1=ALU.add)])
            retire()

        layer_norm("ln1")
        a_mm, a_cp2, a_cp, a_st = (sem(f"attn_{s}") for s in ("multiplied", "rows_copied", "copied", "stored"))
        project("l1_units", ACC, wk1, HT)
        project("l1_src_attn", A1B, ka1B[:], ACC)
        with nc.Block() as block:
            @block.tensor
            def _(pe):
                for i, b in enumerate(range(0, NB, 3)):
                    if i >= 8:
                        pe.wait_ge(a_cp, i - 7)
                    for j in range(min(3, NB - b)):
                        blk = slice((b + j) * P, (b + j + 1) * P)
                        nc.tensor.matmul(ps[i % 8][:, j * (D + 1):j * (D + 1) + D], HT[:, blk], wk1, start=True, stop=True)
                        last = nc.tensor.matmul(ps[i % 8][:, j * (D + 1) + D:(j + 1) * (D + 1)], ACC[:, blk], kaT[:, 1:2],
                                                start=True, stop=True)
                    last.then_inc(a_mm, 1)

            @block.vector
            def _(dve):
                for i, b in enumerate(range(0, NB, 3)):
                    m = min(3, NB - b)
                    dve.wait_ge(a_mm, i + 1)
                    v = ps[i % 8][:, 0:m * (D + 1)].rearrange("p (b d) -> p b d", d=D + 1)
                    nc.vector.tensor_copy(ROWS[:, b:b + m, 0:D], v[:, :, 0:D]).then_inc(a_cp2, 1)
                    nc.vector.tensor_copy(ROWS[:, b:b + m, D + 1:D + 2], v[:, :, D:D + 1]).then_inc(a_cp, 1)
                nc.vector.memset(ROWS[:, :, D:D + 1], 1.0).then_inc(a_cp, 1)

            @block.sync
            def _(sp):
                sp.wait_ge(a_cp, -(-NB // 3) + 1)
                sp.wait_ge(a_cp2, -(-NB // 3))
                tv = t_l1.rearrange("(b p) d -> p b d", p=P)
                sp.dma_start(tv, ROWS[:, :, :]).then_inc(a_st, 16)
                sp.wait_ge(a_st, 16)

        retire()
        CIN = BIG[:, 0:NP].bitcast(FP16).rearrange("p (s n) -> p s n", s=2)
        ZERO = BIG[:, NP:NP + 512]
        HN = NPAIR // 2
        DB, CHB = NSC, SRC_CH // P
        d_cin, d_win, d_a2, d_free = (pair(f"l1d_{s}") for s in ("counts_in", "window", "attn_scaled", "pair_done"))
        d_e, d_m, d_s, d_o = (pair(f"l1d_{s}") for s in ("exps", "maxed", "scored", "summed"))
        d_reset, d_upd, d_open, d_zero, d_go, d_out = (sem(f"l1d_{s}") for s in ("reset", "windows", "round", "zero", "go", "out"))

        def place(b):
            if b < NB - 1:
                return [(b // 3, (b % 3) * (D + 1), 0, D + 1)]
            return [(0, 3 * (D + 1), 0, 512 - 3 * (D + 1)), (1, 3 * (D + 1), 512 - 3 * (D + 1), D + 1)]

        with nc.Block() as block:
            @block.sync
            def _(sp):
                sp.wait_ge(d_open, 1)
                with sp.Fori(0, HN) as i:
                    for s in range(2):
                        sp.wait_ge(d_free[s], i + 1)
                        sp.sem_inc(d_go, 1)
                        sp.dma_start(CIN[:, s, :], counts[bass.ds(2 * i + s, 1), :, :].rearrange("g p n -> p (g n)")).then_inc(d_cin[s], 16)
                        for h in range(2):
                            b = sp.value_load(basei[0:1, bass.ds(4 * i + 2 * s + h, 1)], min_val=0, max_val=LAST)
                            sp.dma_start(hwin[h * W:(h + 1) * W, s, :], t_l1[bass.ds(b, W), :]).then_inc(d_win[s], 16)

            @block.scalar
            def _(act):
                ahead(act, d_free[0])
                with act.Fori(0, HN) as i:
                    for j in range(2 * DB):
                        s, c, q = j // DB, j % DB, j % 2
                        u = i * DB + j // 2
                        if c == 0:
                            act.wait_ge(d_win[s], 32 * i + 32)
                            nc.scalar.activation(st_a2[:, s:s + 1], hwin[:, s, D + 1:D + 2], ACT.Copy, scale=0.2).then_inc(d_a2[s], 1)
                            act.wait_ge(d_a2[s], i + 1)
                        col = slice(c * SRC_CH, (c + 1) * SRC_CH)
                        act.wait_ge(d_m[q], u + 1)
                        nc.scalar.activation(E1[:, q, :], A1B[:, col], ACT.Exp, bias=hwin[:, s, D + 1:D + 2]).then_inc(d_e[q], 1)
                        nc.scalar.activation(E2[:, q, :], A1B[:, col], ACT.Exp, bias=st_a2[:, s:s + 1], scale=0.2).then_inc(d_e[q], 1)
                        if j == DB:
                            act.wait_ge(d_o[0], i * DB + DB // 2 + 2)
                            act.sem_inc(d_free[0], 1)
                        if j == 1:
                            act.wait_ge(d_o[1], i * DB + 1)
                            act.sem_inc(d_free[1], 1)

            @block.vector
            def _(dve):
                ahead(dve, *d_m)
                nc.vector.memset(ZERO, 0.0).then_inc(d_zero, 1)
                round_reset(dve, d_reset)
                round_setup(dve, [d_upd, d_open], 0)
                with dve.Fori(0, HN) as i:
                    for j in range(2 * DB):
                        s, c, q = j // DB, j % DB, j % 2
                        u = i * DB + j // 2
                        dve.wait_ge(d_e[q], 2 * u + 2)
                        dve.wait_ge(d_o[q], u + 1)
                        nc.vector.scalar_tensor_tensor(out=SM[:, q, :], in0=E2[:, q, :], scalar=E_MIN, in1=E1[:, q, :],
                                                       op0=ALU.max, op1=ALU.max).then_inc(d_m[q], 1)
                        dve.wait_ge(d_m[q], u + 2)
                        if c == 0:
                            dve.wait_ge(d_cin[s], 16 * i + 16)
                        nc.vector.scalar_tensor_tensor(out=SM[:, q, :], in0=SM[:, q, :], scalar=E_MAX, in1=CIN[:, s, c * SRC_CH:(c + 1) * SRC_CH],
                                                       op0=ALU.min, op1=ALU.mult).then_inc(d_s[q], 1)
                dve.wait_ge(d_o[0], HN * DB + 1)
                dve.wait_ge(d_o[1], HN * DB + 1)
                for b in range(NB):
                    for bank, at, lo, hi in place(b):
                        nc.vector.tensor_copy(OACC[:, b, lo:hi], ps[bank][:, at:at + hi - lo]).then_inc(d_out, 1)

            @block.tensor
            def _(pe):
                ahead(pe, *d_o)
                pe.wait_ge(d_zero, 1)
                for b in range(8):
                    nc.tensor.matmul(ps[b], ZERO[:, 0:P], ZERO, start=True, stop=False, skip_group_check=True)
                with pe.Fori(0, HN) as i:
                    for j in range(2 * DB):
                        s, c, q = j // DB, j % DB, j % 2
                        u = i * DB + j // 2
                        if c == 0:
                            pe.wait_ge(d_win[s], 32 * i + 32)
                        pe.wait_ge(d_s[q], u + 1)
                        for b in range(CHB):
                            for bank, at, lo, hi in place(c * CHB + b):
                                last = nc.tensor.matmul(ps[bank][:, at:at + hi - lo], SM[:, q, b * P:(b + 1) * P], hwin[:, s, lo:hi],
                                                        start=False, stop=False, skip_group_check=True)
                        last.then_inc(d_o[q], 1)
        retire()

        G_PAIRS = NG // 4
        USES = NSC
        s_st, s_win, s_ohd, s_gp = (pair(f"l1_{s}") for s in ("staged", "window", "dst_onehot", "pair_done"))
        s_osd, s_c, s_e, s_m, s_s, s_o, s_add = (
            pair(f"l1_{s}") for s in ("src_onehot", "counted", "exps", "maxed",
                                      "scored", "summed", "added"))
        s_rel = pair("l1_rel_staged")
        upd, opened = sem("l1_windows"), sem("l1_round")
        win_go = sem("l1_window_go")

        def chunks(body):
            for j in range(2 * NSC):
                body(j // NSC, j % NSC, j % 2, j // 2)

        with nc.Block() as block:
            @block.sync
            def _(sp):
                R = reg_rounds(sp)
                with sp.If(R > 1), sp.Fori(0, R - 1) as r:
                    with sp.Fori(0, G_PAIRS) as i:
                        n = r * G_PAIRS + i
                        sp.wait_ge(opened, r + 1)
                        sp.sem_inc(win_go, 1)
                        for s in range(2):
                            sp.wait_ge(s_gp[s], n + 1)
                            sp.sem_inc(win_go, 1)
                            for h in range(2):
                                b = sp.value_load(basei[0:1, bass.ds(4 * i + 2 * s + h, 1)], min_val=0, max_val=LAST)
                                sp.dma_start(hwin[h * W:(h + 1) * W, s, :], t_l1[bass.ds(b, W), :]).then_inc(s_win[s], 16)

            @block.scalar
            def _(act):
                R = reg_rounds(act)
                with act.If(R > 1), act.Fori(0, R - 1) as r:
                    with act.Fori(0, G_PAIRS) as i:
                        n = r * G_PAIRS + i
                        act.wait_ge(opened, r + 1)

                        def stage(s):
                            act.wait_ge(s_gp[s], n + 1)
                            g = bass.ds(4 * i + 2 * s, 2)
                            nc.scalar.copy(st_src[:, s, :].rearrange("p (g t) -> p g t", g=2), srcF[:, g, :]).then_inc(s_st[s], 1)
                            nc.scalar.copy(st_rel[:, s, :].rearrange("p (g t) -> p g t", g=2), relc[:, g, :]).then_inc(s_rel[s], 1)
                            act.wait_ge(s_win[s], 32 * n + 32)
                            nc.scalar.activation(st_a2[:, s:s + 1], hwin[:, s, D + 1:D + 2], ACT.Copy, scale=0.2).then_inc(s_st[s], 1)

                        def body(s, c, q, u):
                            if c == 0:
                                stage(s)
                            m = n * USES + u
                            col = slice(c * SRC_CH, (c + 1) * SRC_CH)
                            act.wait_ge(s_m[q], m + 1)
                            if c == 0:
                                act.wait_ge(s_st[s], 2 * n + 2)
                            nc.scalar.activation(E1[:, q, :], A1B[:, col], ACT.Exp, bias=hwin[:, s, D + 1:D + 2]).then_inc(s_e[q], 1)
                            nc.scalar.activation(E2[:, q, :], A1B[:, col], ACT.Exp, bias=st_a2[:, s:s + 1], scale=0.2).then_inc(s_e[q], 1)
                        chunks(body)

            @block.vector
            def _(dve):
                ahead(dve, *s_gp, *s_s, *s_add, *s_m)
                R = reg_rounds(dve)
                with dve.If(R > 1), dve.Fori(0, R - 1) as r:
                    round_setup(dve, [upd, opened], r)
                    with dve.Fori(0, G_PAIRS) as i:
                        n = r * G_PAIRS + i

                        def dst_onehot(s):
                            dve.wait_ge(s_rel[s], n + 1)
                            dve.wait_ge(s_gp[s], n + 1)
                            pair_dst_onehot(s, s_ohd[s])

                        def src_onehot(s, c, q, u):
                            m = n * USES + u
                            if c == 0:
                                dst_onehot(s)
                                dve.wait_ge(s_st[s], 2 * n + 1)
                            dve.wait_ge(s_c[q], m + 1)
                            for t in range(16):
                                last = nc.vector.tensor_scalar(OHS[:, q, t, :], iotaS[:], st_src[:, s, t:t + 1], -float(c * SRC_CH),
                                                               ALU.subtract, ALU.is_equal)
                            last.then_inc(s_osd[q], 1)

                        def score(s, c, q, u):
                            m = n * USES + u
                            dve.wait_ge(s_e[q], 2 * m + 2)
                            dve.wait_ge(s_o[q], m + 1)
                            nc.vector.scalar_tensor_tensor(out=SM[:, q, :], in0=E2[:, q, :], scalar=E_MIN, in1=E1[:, q, :],
                                                           op0=ALU.max, op1=ALU.max).then_inc(s_m[q], 1)
                            dve.wait_ge(s_m[q], m + 2)
                            dve.wait_ge(s_c[q], m + 2)
                            nc.vector.scalar_tensor_tensor(out=SM[:, q, :].rearrange("p (a s) -> p a s", a=2),
                                                           in0=SM[:, q, :].rearrange("p (a s) -> p a s", a=2), scalar=E_MAX,
                                                           in1=C_PS[q][:, :, 0:HALF], op0=ALU.min, op1=ALU.mult).then_inc(s_s[q], 1)

                        def add(s, c, q, u):
                            m = n * USES + u
                            dve.wait_ge(s_o[q], m + 2)
                            b = c * SBLK
                            first = nc.vector.tensor_tensor(OACC[:, b:b + 3, 0:D + 1], OACC[:, b:b + 3, 0:D + 1],
                                                            O_PS[q][:, 0, 0:3 * (D + 1)].rearrange("p (b d) -> p b d", d=D + 1), ALU.add)
                            if c == NSC - 1:
                                first.then_inc(s_gp[s], 1)
                            nc.vector.tensor_tensor(OACC[:, b + 3:b + 5, 0:D + 1], OACC[:, b + 3:b + 5, 0:D + 1],
                                                    O_PS[q][:, 1, 0:2 * (D + 1)].rearrange("p (b d) -> p b d", d=D + 1),
                                                    ALU.add).then_inc(s_add[q], 1)

                        every = []
                        chunks(lambda *a: every.append(a))
                        src_onehot(*every[0])
                        for j, a in enumerate(every):
                            if j + 1 < len(every):
                                src_onehot(*every[j + 1])
                            score(*a)
                            if j:
                                add(*every[j - 1])
                        add(*every[-1])

            @block.tensor
            def _(pe):
                ahead(pe, *s_c, *s_o)
                R = reg_rounds(pe)
                with pe.If(R > 1), pe.Fori(0, R - 1) as r:
                    with pe.Fori(0, G_PAIRS) as i:
                        n = r * G_PAIRS + i

                        def count(s, c, q, u):
                            m = n * USES + u
                            if c == 0:
                                pe.wait_ge(s_ohd[s], 2 * n + 2)
                            pe.wait_ge(s_s[q], m + 1)
                            pe.wait_ge(s_osd[q], m + 1)
                            for h in range(2):
                                for t in range(16):
                                    last = nc.tensor.matmul(C_PS[q][:, h, 0:HALF], OHD[:, s, t, :],
                                                            OHS[:, q, t, h * HALF:(h + 1) * HALF], start=(t == 0), stop=(t == 15))
                            last.then_inc(s_c[q], 1)

                        def weigh(s, c, q, u):
                            m = n * USES + u
                            if c == 0:
                                pe.wait_ge(s_win[s], 32 * n + 32)
                            pe.wait_ge(s_add[q], m + 1)
                            pe.wait_ge(s_s[q], m + 2)
                            for b in range(SBLK):
                                last = nc.tensor.matmul(O_PS[q][:, b // 3, (b % 3) * (D + 1):(b % 3 + 1) * (D + 1)],
                                                        SM[:, q, b * P:(b + 1) * P], hwin[:, s, 0:D + 1], start=True, stop=True)
                            last.then_inc(s_o[q], 1)

                        every = []
                        chunks(lambda *a: every.append(a))
                        count(*every[0])
                        for j, a in enumerate(every):
                            if j + 1 < len(every):
                                count(*every[j + 1])
                            weigh(*a)

        l1_n, l1_tr, l1_add = sem("l1_normed"), sem("l1_transposed"), sem("l1_residual")
        with nc.Block() as block:
            @block.vector
            def _(dve):
                den = OACC[:, :, D:D + 1]
                nc.vector.tensor_scalar(den, den, 1e-6, None, ALU.max).then_inc(l1_n, 1)
                dve.wait_ge(l1_n, 1)
                nc.vector.reciprocal(den, den).then_inc(l1_n, 1)
                dve.wait_ge(l1_n, 2)
                nc.vector.tensor_tensor(OACC[:, :, 0:D], OACC[:, :, 0:D], den.to_broadcast([P, NB, D]), ALU.mult).then_inc(l1_n, 1)
                for i, b in enumerate(range(0, NB, 4)):
                    m = min(4, NB - b)
                    dve.wait_ge(l1_tr, i + 1)
                    nc.vector.tensor_tensor(XT[:, b * P:(b + m) * P], XT[:, b * P:(b + m) * P], ps[i][:, 0:m * P], ALU.add).then_inc(l1_add, 1)

            @block.tensor
            def _(pe):
                pe.wait_ge(l1_n, 3)
                for i, b in enumerate(range(0, NB, 4)):
                    for j in range(min(4, NB - b)):
                        last = nc.tensor.transpose(ps[i][:, j * P:(j + 1) * P], OACC[:, b + j, 0:D], ident[:])
                    last.then_inc(l1_tr, 1)

        retire()
        if STOP >= 2:
            layer_norm("ln2")
            q_st = store_rows("l2_q", HT, wq, t_q)
            kv_st = store_rows("l2_kv", HT, wkv.rearrange("p a d -> p (a d)"), t_kv, 2 * D)
            on_vector("l2_start", [lambda: V.memset(ACC[:], 0.0), lambda: V.memset(ACC2[:], 0.0),
                                   lambda: V.memset(QW[:], 0.0)])
            SL, SU = 4, 2
            NI4 = NG // SL

            def four(name):
                return [sem(f"{name}{k}") for k in range(SL)]

            s_idx, s_g, s_q, s_oh, s_fin = (four(f"l2_{s}") for s in ("index", "gathered", "qwin", "onehot", "summed"))
            s_pt, s_oht, s_qg, s_pr, s_ex, s_msg, s_ev, s_evz = (
                pair(f"l2_{s}") for s in ("transposed", "onehot_t", "q_gathered", "score", "exp", "msg", "added", "z_added"))
            reset2, upd2, opened2 = sem("l2_reset"), sem("l2_windows"), sem("l2_round")
            qwin_go, kv_go = sem("l2_window_go"), sem("l2_gather_go")
            with nc.Block() as block:
                @block.sync
                def _(sp):
                    R = reg_rounds(sp)
                    with sp.Fori(0, R) as r:
                        with sp.Fori(0, NI4) as i:
                            n = r * NI4 + i
                            sp.wait_ge(opened2, r + 1)
                            sp.sem_inc(qwin_go, 1)
                            for k in range(SL):
                                b = sp.value_load(basei[0:1, bass.ds(SL * i + k, 1)], min_val=0, max_val=LAST)
                                sp.wait_ge(s_fin[k], n + 1)
                                for a in range(2):
                                    sp.dma_start(QW[a * W:(a + 1) * W, k, a * D:(a + 1) * D], t_q[bass.ds(b, W), :]).then_inc(s_q[k], 16)
                                if k < SL - 1:
                                    sp.sem_inc(qwin_go, 1)

                @block.gpsimd
                def _(pool):
                    R = reg_rounds(pool)
                    with pool.Fori(0, R) as r:
                        with pool.Fori(0, NI4) as i:
                            n = r * NI4 + i
                            for k in range(SL):
                                pool.wait_ge(s_fin[k], n + 1)
                                pool.sem_inc(kv_go, 1)
                                nc.gpsimd.tensor_copy(idx[:, k, :], srcI[:, bass.ds(SL * i + k, 1), :]).then_inc(s_idx[k], 1)
                                pool.wait_ge(s_idx[k], n + 1)
                                pool.sem_inc(kv_go, 1)
                                for t in range(TILES):
                                    pool.indirect_dma_start(
                                        out=G1KV[:, k, t, :], out_offset=None, in_=t_kv,
                                        in_offset=bass.IndirectOffsetOnAxis(ap=idx[:, k, t:t + 1], axis=0),
                                    ).then_inc(s_g[k], 16)

                @block.scalar
                def _(act):
                    ahead(act, *s_ex, *s_oht)
                    R = reg_rounds(act)
                    with act.Fori(0, R) as r:
                        with act.Fori(0, NI4) as i:
                            n = r * NI4 + i

                            def onehot_t(k):
                                q, u = k % 2, n * SU + k // 2
                                act.wait_ge(s_pt[q], u + 1)
                                act.wait_ge(s_qg[q], u + 1)
                                nc.scalar.copy(OHT[:, q, :, :], ps[q][:, :].rearrange("p (t e) -> p t e", t=4)).then_inc(s_oht[q], 1)

                            def exps(k):
                                q, u = k % 2, n * SU + k // 2
                                if k >= 2:
                                    act.wait_ge(s_fin[k - 2], n + 2)
                                else:
                                    act.wait_ge(s_fin[k + 2], n + 1)
                                act.wait_ge(s_pr[q], 4 * u + 4)
                                nc.scalar.activation(SX[:, q, :].rearrange("p (h d) -> p h d", d=DH),
                                                     SC[:, q, 2, :, None].to_broadcast([P, TILES * HEADS, DH]), ACT.Exp).then_inc(s_ex[q], 1)

                            onehot_t(0)
                            onehot_t(1)
                            exps(0)
                            onehot_t(2)
                            exps(1)
                            onehot_t(3)
                            exps(2)
                            exps(3)

                @block.vector
                def _(dve):
                    ahead(dve, *s_msg, *s_ev)
                    R = reg_rounds(dve)
                    round_reset(dve, reset2)
                    with dve.Fori(0, R) as r:
                        round_setup(dve, [upd2, opened2], r)
                        with dve.Fori(0, NI4) as i:
                            n = r * NI4 + i

                            def messages(k):
                                q, u = k % 2, n * SU + k // 2
                                dve.wait_ge(s_g[k], n * (16 * TILES) + 16 * TILES)
                                dve.wait_ge(s_qg[q], u + 2)
                                dve.wait_ge(s_ex[q], u + 1)
                                nc.vector.tensor_tensor(PR[:, :, :].rearrange("p (h t) d -> p h (t d)", h=2),
                                                        G1KV[:, k, :, 0:D].rearrange("p (h t) d -> p h t d", h=2),
                                                        big_ps[:, 2 + 2 * q:4 + 2 * q, :].rearrange("p h (t d) -> p h t d", t=4),
                                                        ALU.mult).then_inc(s_pr[q], 1)
                                dve.wait_ge(s_pr[q], 4 * u + 1)
                                nc.vector.tensor_reduce(SC[:, q, 0, :], PR[:, :, :].rearrange("p t (h d) -> p (t h) d", d=DH),
                                                        AX_X, ALU.add).then_inc(s_pr[q], 1)
                                dve.wait_ge(s_pr[q], 4 * u + 2)
                                nc.vector.tensor_tensor(SC[:, q, 1, :].rearrange("p (t h) -> p t h", h=HEADS), SC[:, q, 0, :].rearrange("p (t h) -> p t h", h=HEADS),
                                                        attr[:, bass.ds(SL * i + k, 1), :].rearrange("p g t -> p (g t)")[:, :, None].to_broadcast([P, TILES, HEADS]),
                                                        ALU.mult).then_inc(s_pr[q], 1)
                                dve.wait_ge(s_pr[q], 4 * u + 3)
                                nc.vector.tensor_scalar(SC[:, q, 2, :], SC[:, q, 1, :], 5.0, -5.0, ALU.min, ALU.max).then_inc(s_pr[q], 1)

                            def weigh(k):
                                q, u = k % 2, n * SU + k // 2
                                dve.wait_ge(s_ex[q], u + 2)
                                nc.vector.tensor_tensor(MSG[:, q, :].rearrange("p (t d) -> p t d", t=TILES), G1KV[:, k, :, D:2 * D],
                                                        SX[:, q, :].rearrange("p (t d) -> p t d", t=TILES), ALU.mult).then_inc(s_msg[q], 1)

                            def add(k):
                                q, u = k % 2, n * SU + k // 2
                                b = dve.value_load(basei[0:1, bass.ds(SL * i + k, 1)], min_val=0, max_val=LAST)
                                dve.wait_ge(s_ev[1 - q], u + 1 + q)
                                dve.wait_ge(s_fin[k], n + 2)
                                nc.vector.tensor_tensor(ACC[:, bass.ds(b, W)], ACC[:, bass.ds(b, W)], ps[6 + q][:, 0:W], ALU.add).then_inc(s_evz[q], 1)
                                nc.vector.tensor_tensor(ACC2[:, bass.ds(b, W)], ACC2[:, bass.ds(b, W)], ps[6 + q][:, W:2 * W], ALU.add).then_inc(s_ev[q], 1)

                            for k in range(SL):
                                dve.wait_ge(s_fin[k], n + 1)
                                nc.vector.tensor_tensor(
                                    OH[:, k, :, :], iota64[:, None, :].to_broadcast([P, TILES, W]),
                                    relc[:, bass.ds(SL * i + k, 1), :].rearrange("p g t -> p (g t)")[:, :, None].to_broadcast([P, TILES, W]),
                                    ALU.is_equal).then_inc(s_oh[k], 1)
                            for k in range(SL):
                                messages(k)
                                if k:
                                    add(k - 1)
                                weigh(k)
                            add(SL - 1)

                @block.tensor
                def _(pe):
                    ahead(pe, *s_fin, *s_qg)
                    R = reg_rounds(pe)
                    with pe.Fori(0, R) as r:
                        with pe.Fori(0, NI4) as i:
                            n = r * NI4 + i

                            def pick_q(k):
                                q, u = k % 2, n * SU + k // 2
                                pe.wait_ge(s_oh[k], n + 1)
                                pe.wait_ge(s_oht[q], u + 1)
                                for t in range(4):
                                    last = nc.tensor.transpose(ps[q][:, t * P:(t + 1) * P], OH[:, k, 2 * t:2 * t + 2, :].rearrange("p t w -> p (t w)"), ident[:])
                                last.then_inc(s_pt[q], 1)
                                pe.wait_ge(s_q[k], 32 * n + 32)
                                pe.wait_ge(s_msg[q], u + 1)
                                pe.wait_ge(s_oht[q], u + 2)
                                for t in range(4):
                                    last = nc.tensor.matmul(ps[2 + 2 * q + t // 2][:, (t % 2) * 2 * D:(t % 2 + 1) * 2 * D], OHT[:, q, t, :],
                                                            QW[:, k, :], start=True, stop=True)
                                last.then_inc(s_qg[q], 1)

                            def sums(k):
                                q, u = k % 2, n * SU + k // 2
                                pe.wait_ge(s_ev[q], u + 1)
                                pe.wait_ge(s_msg[q], u + 2)
                                for a, src_ in ((0, MSG), (1, SX)):
                                    for t in range(TILES):
                                        last = nc.tensor.matmul(ps[6 + q][:, a * W:(a + 1) * W], src_[:, q, t * D:(t + 1) * D], OH[:, k, t, :],
                                                                start=(t == 0), stop=(t == TILES - 1))
                                last.then_inc(s_fin[k], 1)

                            pick_q(0)
                            pick_q(1)
                            for k in range(SL):
                                sums(k)
                                if k + 2 < SL:
                                    pick_q(k + 2)

            on_vector("l2_div", [lambda: V.tensor_scalar(ACC2[:], ACC2[:], 1e-6, None, ALU.add),
                                 lambda: V.reciprocal(ACC2[:], ACC2[:]),
                                 lambda: V.tensor_tensor(ACC[:], ACC[:], ACC2[:], ALU.mult)])
            project("l2_o", TMP, wo, ACC)

            def batch_norm(name, T, S2, gamma, beta):
                s = sem(name)
                st8 = lambda j: stat[:, j:j + 1]
                with nc.Block() as block:
                    @block.vector
                    def _(dve):
                        steps = [
                            lambda: V.tensor_reduce(st8(0), T[:, 0:N], AX_X, ALU.add),
                            lambda: V.tensor_scalar(st8(0), st8(0), 1.0 / N, None, ALU.mult),
                            lambda: V.tensor_scalar(T[:], T[:], st8(0), None, ALU.subtract),
                            lambda: V.tensor_tensor(S2[:], T[:], T[:], ALU.mult),
                            lambda: V.tensor_reduce(st8(1), S2[:, 0:N], AX_X, ALU.add),
                            lambda: V.tensor_scalar(st8(1), st8(1), 1.0 / N, EPS, ALU.mult, ALU.add)]
                        for i, st_ in enumerate(steps):
                            if i:
                                dve.wait_ge(s, i)
                            st_().then_inc(s, 1)
                        dve.wait_ge(s, 7)
                        V.reciprocal(st8(3), st8(2)).then_inc(s, 1)
                        dve.wait_ge(s, 8)
                        V.tensor_tensor(st8(4), st8(3), vec[:, gamma:gamma + 1], ALU.mult).then_inc(s, 1)
                        dve.wait_ge(s, 9)
                        V.tensor_scalar(T[:], T[:], st8(4), vec[:, beta:beta + 1], ALU.mult, ALU.add).then_inc(s, 1)

                    @block.scalar
                    def _(act):
                        act.wait_ge(s, 6)
                        nc.scalar.activation(st8(2), st8(1), ACT.Sqrt).then_inc(s, 1)

            on_vector("l2_res", [lambda: V.scalar_tensor_tensor(out=TMP[:], in0=TMP[:], scalar=vec[:, BO:BO + 1], in1=HT[:],
                                                                op0=ALU.add, op1=ALU.add)])
            batch_norm("l2_bn1", TMP, HT, G1, BB1)
            for a, hid in ((0, HT), (1, ACC)):
                project(f"l2_f1_{a}", hid, f1[:, a * D:(a + 1) * D], TMP)
                on_vector(f"l2_relu_{a}", [lambda: V.tensor_scalar(hid[:], hid[:], vec[:, BF1 + a:BF1 + a + 1], 0.0, ALU.add, ALU.max)])
            f_mm, f_add = sem("l2_f2_multiplied"), sem("l2_f2_added")
            with nc.Block() as block:
                @block.tensor
                def _(pe):
                    for c in range(NC):
                        nc.tensor.matmul(ps[c][:, 0:CH], f2[:, 0, :], chunk(HT, c), start=True, stop=False)
                        nc.tensor.matmul(ps[c][:, 0:CH], f2[:, 1, :], chunk(ACC, c), start=False, stop=True).then_inc(f_mm, 1)

                @block.vector
                def _(dve):
                    for c in range(NC):
                        dve.wait_ge(f_mm, c + 1)
                        V.scalar_tensor_tensor(out=chunk(TMP, c), in0=ps[c][:, 0:CH], scalar=vec[:, BF2:BF2 + 1], in1=chunk(TMP, c),
                                               op0=ALU.add, op1=ALU.add).then_inc(f_add, 1)
            batch_norm("l2_bn2", TMP, HT, G2, BB2)
            on_vector("l2_end", [lambda: V.tensor_tensor(XT[:], XT[:], TMP[:], ALU.add)])

        retire()
        if STOP >= 3:
            layer_norm("ln3")
            on_vector("l3_start", [lambda: V.memset(ACC[:], 0.0)])
            store_rows("l3_rows", HT, ident[:], t_l3)
            aggregate("l3_sum", t_l3, wgt3, ACC)
            on_vector("l3_end", [lambda: V.tensor_tensor(XT[:], XT[:], ACC[:], ALU.add)])

        o_tr, o_cp, o_st = sem("out_transposed"), sem("out_copied"), sem("out_stored")
        with nc.Block() as block:
            @block.tensor
            def _(pe):
                for i, b in enumerate(range(0, NB, 4)):
                    for j in range(min(4, NB - b)):
                        last = nc.tensor.transpose(ps[i][:, j * P:(j + 1) * P], XT[:, (b + j) * P:(b + j + 1) * P], ident[:])
                    last.then_inc(o_tr, 1)

            @block.vector
            def _(dve):
                for i, b in enumerate(range(0, NB, 4)):
                    m = min(4, NB - b)
                    dve.wait_ge(o_tr, i + 1)
                    nc.vector.tensor_copy(ROWS[:, b:b + m, 0:D], ps[i][:, 0:m * P].rearrange("p (b d) -> p b d", d=D)).then_inc(o_cp, 1)

            @block.sync
            def _(sp):
                sp.wait_ge(o_cp, 7)
                sp.dma_start(out[0:(NB - 1) * P, :].rearrange("(b p) d -> p b d", p=P), ROWS[:, 0:NB - 1, 0:D]).then_inc(o_st, 16)
                sp.dma_start(out[(NB - 1) * P:N, :], ROWS[0:N - (NB - 1) * P, NB - 1, 0:D]).then_inc(o_st, 16)
                sp.wait_ge(o_st, 32)


STOP = 3


_INS = ['x', 'src', 'dst', 'edge_weight', 'edge_weight_n2', 'edge_weight1', 'L0_gnn_W0', 'L0_gnn_b0', 'L0_gnn_W1',
        'L0_gnn_b1', 'L0_gnn_W2', 'L0_gnn_b2', 'L1_gnn_kernel', 'L1_gnn_kernel_attention', 'L2_gnn_Wq', 'L2_gnn_Wk',
        'L2_gnn_We', 'L2_gnn_Wv', 'L2_gnn_Wo', 'L2_gnn_bo', 'L2_gnn_g1', 'L2_gnn_b1', 'L2_gnn_W1', 'L2_gnn_bf1',
        'L2_gnn_W2', 'L2_gnn_bf2', 'L2_gnn_g2', 'L2_gnn_b2', 'L3_gnn_decay_lam']


def kernel(**inputs):
    import numpy as _np
    import concourse.bacc as _bacc
    from concourse import mybir as _mybir
    from concourse.bass_utils import run_bass_kernel_spmd as _run

    nc = _bacc.Bacc("TRN2", target_bir_lowering=False, num_devices=1)
    arrays, args = {}, []
    for name in _INS:
        a = _np.ascontiguousarray(inputs[name])
        arrays[f"in_{name}"] = a
        args.append(nc.dram_tensor(f"in_{name}", a.shape, _mybir.dt.from_np(a.dtype), kind="ExternalInput").ap())
    args.append(nc.dram_tensor("out_0", (N, D), _mybir.dt.from_np(_np.dtype("float32")), kind="ExternalOutput").ap())
    gnn(nc, *args)
    r = _run(nc, [arrays], core_ids=[0])
    return r.results[0]["out_0"]
```
